# Optimizing a Trainium2 kernel written in Bass

```python
import numpy as np
import jax
import jax.numpy as jnp

def _softmax(x, axis=-1):
    return jax.nn.softmax(x, axis=axis)
def _gelu(x):
    return jax.nn.gelu(x, approximate=True)
def _silu(x):
    return jax.nn.silu(x)
def _sigmoid(x):
    return jax.nn.sigmoid(x)
def _layernorm(x, axis=-1, eps=1e-5):
    m = jnp.mean(x, axis=axis, keepdims=True)
    v = jnp.var(x, axis=axis, keepdims=True)
    return (x - m) / jnp.sqrt(v + eps)
def _scatter_add(tgt, idx, src, axis=0):
    return tgt.at[idx].add(src)
def _segment_sum(src, seg, n):
    return jax.ops.segment_sum(src, seg, n)

kernel_name = 'mk_conv_preact_d1_conv_nchw64_92bac9'

def setup_inputs(seed: int = 0):
    np.random.seed(seed)
    _w = jnp.asarray
    def _rec_inputs():
        import jax
        import jax.numpy as jnp
        _gk = jax.random.key(seed)
        x = -0.000125 + 0.9999 * jax.random.normal(jax.random.fold_in(_gk, 1), (8, 64, 256, 256), jnp.float32)
        return x
    x = _rec_inputs()
    def _L0_conv_setup():
        import jax, jax.numpy as jnp
        import numpy as np
        P = 4
        key = jax.random.key(seed)
        k = jax.random.split(key, 6)
        B, C, H, W, HID = (8, 64, 256, 256, 256)
        return {'x': jax.random.normal(k[0], (B, C, H, W), dtype=jnp.float32), 'w1': jax.random.normal(k[1], (HID, C), dtype=jnp.float32) * 0.05, 'b1': jax.random.normal(k[2], (HID,), dtype=jnp.float32) * 0.05, 'w2': jax.random.normal(k[3], (C, HID), dtype=jnp.float32) * 0.05, 'b2': jax.random.normal(k[4], (C,), dtype=jnp.float32) * 0.05, 'cweight': jax.random.normal(k[5], (P, P // 2 + 1, C, 2), dtype=jnp.float32)}
    _L0_conv_all = _L0_conv_setup()
    _L0_conv_in = {k: v for k, v in _L0_conv_all.items() if k in ('w1', 'b1', 'w2', 'b2', 'cweight', )}
    del _L0_conv_all

    return {
        "x": x,
        "L0_conv_w1": _L0_conv_in["w1"],
        "L0_conv_b1": _L0_conv_in["b1"],
        "L0_conv_w2": _L0_conv_in["w2"],
        "L0_conv_b2": _L0_conv_in["b2"],
        "L0_conv_cweight": _L0_conv_in["cweight"],
    }

def reference(x, L0_conv_w1, L0_conv_b1, L0_conv_w2, L0_conv_b2, L0_conv_cweight):
    import jax
    import jax.numpy as jnp
    def _L0_conv_ref(x, w1, b1, w2, b2, cweight):
        import jax, jax.numpy as jnp
        import numpy as np
        P = 4
        h = jnp.einsum('bchw,oc->bohw', x, w1) + b1[None, :, None, None]
        h = jax.nn.gelu(h, approximate=False)
        y = jnp.einsum('bchw,oc->bohw', h, w2) + b2[None, :, None, None]
        b, c, H, W = y.shape
        y = y.reshape(b, c, H // P, P, W // P, P).transpose(0, 2, 4, 3, 5, 1)
        yf = jnp.fft.rfft2(y.astype(jnp.float32), axes=(3, 4), norm='ortho')
        w = cweight[..., 0] + 1j * cweight[..., 1]
        yf = yf * w
        y = jnp.fft.irfft2(yf, s=(P, P), axes=(3, 4), norm='ortho')
        y = y.transpose(0, 5, 1, 3, 2, 4).reshape(b, c, H, W)
        return y.astype(x.dtype)

    def _gn(v, G=32, eps=1e-5):
        B_, C_, H_, W_ = v.shape
        g = v.reshape(B_, G, C_ // G, H_, W_)
        m = jnp.mean(g, axis=(2, 3, 4), keepdims=True)
        s = jnp.var(g, axis=(2, 3, 4), keepdims=True)
        return ((g - m) / jnp.sqrt(s + eps)).reshape(v.shape)

    def _ln_c(v, eps=1e-6):
        m = jnp.mean(v, axis=1, keepdims=True)
        s = jnp.var(v, axis=1, keepdims=True)
        return (v - m) / jnp.sqrt(s + eps)

    def _ln_t(v, eps=1e-5):
        m = jnp.mean(v, axis=-1, keepdims=True)
        s = jnp.var(v, axis=-1, keepdims=True)
        return (v - m) / jnp.sqrt(s + eps)

    def _to_tokens(v):
        B_, C_, H_, W_ = v.shape
        return v.reshape(B_, C_, H_ * W_).transpose(0, 2, 1)
    def _from_tokens(t, like):
        B_, C_, H_, W_ = like.shape
        return t.transpose(0, 2, 1).reshape(B_, C_, H_, W_)

    x = x + _L0_conv_ref(_gn(x), L0_conv_w1, L0_conv_b1, L0_conv_w2, L0_conv_b2, L0_conv_cweight)
    return x


_drawn_inputs = setup_inputs


def setup_inputs(seed=0):
    import zlib

    import numpy as np

    out = dict(_drawn_inputs(seed))
    spreads = {}
    factors = {}
    for name, (base, spread) in spreads.items():
        noise = np.random.default_rng([zlib.crc32(name.encode()), seed]).standard_normal(out[name].shape)
        drawn = base * np.exp(spread * noise) if base else spread * noise
        out[name] = jnp.asarray(drawn.astype(out[name].dtype))
    for name, factor in factors.items():
        out[name] = (out[name] * factor).astype(out[name].dtype)
    return out
```

```python
from contextlib import ExitStack

import numpy as np

import concourse.bass as bass
from concourse import mybir

F32 = mybir.dt.float32
F32R = mybir.dt.float32r
ALU = mybir.AluOpType
ACT = mybir.ActivationFunctionType

B, C, H, W, HID = 8, 64, 256, 256, 256
PATCH = 4
GROUPS = 32
EPS = 1e-5
P = 128
KH = HID // P
NI = 2
ROWS = 2 * PATCH
UW = ROWS // NI * W
CW = UW // 2
UNITS = H // ROWS
PAIRS = UNITS // 2
RING = UNITS + 4
NQ = 2 * (W // PATCH)
STAT = 6
CONSTS = 7
TAPS = 16


def filter_tables():
    table = np.zeros((NI, 24, 2 * TAPS))
    r = np.arange(PATCH)
    for u in range(PATCH):
        for v in range(PATCH // 2 + 1):
            for z in range(2):
                angle = 2 * np.pi * (u * r[:, None] + v * r[None, :]) / PATCH
                taps = (np.cos(angle) if z == 0 else -np.sin(angle)) / PATCH**2
                if v == 1:
                    taps = 2 * taps
                for n in range(TAPS):
                    al, be, t, to = (n >> 3) & 1, (n >> 2) & 1, (n >> 1) & 1, n & 1
                    for i in range(NI):
                        for other in range(2):
                            io = i ^ other
                            d, e = (io - i) & 1, (to - t) & 1
                            sign = (-1) ** (al * (io < i) + be * (to < t))
                            k = sum((-1) ** (al * a + be * s) * taps[d + 2 * a, e + 2 * s]
                                    for a in range(2) for s in range(2))
                            table[i, u * 6 + v * 2 + z, other * TAPS + n] = sign * k / 4
    return np.round(table * 64) / 64


def program(nc, x, w1t, b1t, w2t, b2t, cwt, table, masks, out):
    ctx = ExitStack()
    with ctx:
        def sb(name, shape, dt=F32):
            return ctx.enter_context(nc.sbuf_tensor(name, shape, dt))

        def ps(name, shape):
            return ctx.enter_context(nc.psum_tensor(name, shape, F32))

        def sem(name):
            return ctx.enter_context(nc.semaphore(name))

        ring = sb("ring", [P, RING, UW])
        xhi = sb("xhi", [P, 2, CW], F32R)
        xlo = sb("xlo", [P, 2, CW], F32R)
        hid = sb("hid", [P, 2, KH, NI, CW])
        ycopy = sb("ycopy", [P, 2 * W])
        eo = sb("eo", [P, 2, UW // 2])
        vin = sb("vin", [P, 2, 2, 2, NQ])
        zcopy = sb("zcopy", [P, UW // 2])
        gj = sb("gj", [P, 2, 2, 2, NQ])
        conv = sb("conv", [P, UW])
        taps = sb("taps", [P, TAPS, P])
        w1 = sb("w1", [P, HID])
        w1s = sb("w1s", [P, HID])
        w1hi = sb("w1hi", [P, HID], F32R)
        w1lo = sb("w1lo", [P, HID], F32R)
        w2 = sb("w2", [P, KH, C])
        b1 = sb("b1", [P, KH])
        b2 = sb("b2", [P, 1])
        cw = sb("cw", [24, C])
        tab = sb("tab", [24, NI, 2 * TAPS])
        mask = sb("mask", [P, 2, P])
        diag = sb("diag", [P, 2 * TAPS])
        stats = sb("stats", [P, UNITS, 2 * STAT])
        mv = sb("mv", [P, 2])
        part = sb("part", [P, 1])
        swapped = sb("swapped", [P, 1])
        rows = sb("rows", [P, 1])
        buddy = sb("buddy", [P, 1])
        mean = sb("mean", [P, 1])
        var = sb("var", [P, 1])
        rstd = sb("rstd", [P, 1])
        nhalf = sb("nhalf", [P, 1])

        hps = ps("hps", [P, KH, NI, CW])
        yps = ps("yps", [P, 2, CW])
        zps = ps("zps", [P, 2, 2, 2, NQ])

        consts_in = sem("consts_in")
        x_in = [sem("x_in0"), sem("x_in1")]
        x_out = [sem("x_out0"), sem("x_out1")]
        diag_ready = sem("diag_ready")
        diag_copied = sem("diag_copied")
        taps_made = sem("taps_made")
        staged = sem("staged")
        scaled = sem("scaled")
        mm1_done = sem("mm1_done")
        gelu_done = sem("gelu_done")
        mm2_done = sem("mm2_done")
        ycopied = sem("ycopied")
        y_read = sem("y_read")
        v_ready = sem("v_ready")
        z_ready = sem("z_ready")
        zcopied = sem("zcopied")
        z_read = sem("z_read")
        conv_ready = sem("conv_ready")
        added = sem("added")
        xhi_done = sem("xhi_done")
        var_ready = sem("var_ready")
        rstd_ready = sem("rstd_ready")

        x_v = x.rearrange("n c (u r i) w -> n u i c r w", r=ROWS // NI, i=NI)
        out_v = out.rearrange("n c (u r i) w -> n u i c r w", r=ROWS // NI, i=NI)

        block = ctx.enter_context(nc.Block())

        @block.sync
        def _(sp):
            def place(pair, k):
                values = (pair // PAIRS, 2 * (pair % PAIRS) + k, (2 * pair + k) % RING)
                return [v if isinstance(v, int) else sp.snap(v) for v in values]

            def rows_of_ring(slot, i):
                return ring[i * C:(i + 1) * C, bass.ds(slot, 1), :].rearrange("c o (r w) -> c (o r) w", w=W)

            def load(n, u, slot, k):
                for i in range(NI):
                    sp.dma_start(rows_of_ring(slot, i), x_v[n, u, i]).then_inc(x_in[k], 16)

            def store_half(n, u, slot, k, i):
                sp.dma_start(out_v[n, u, i], rows_of_ring(slot, i)).then_inc(x_out[k], 16)

            for k in range(2):
                load(*place(0, k), k)
            for dst, src in ((w1, w1t), (w2, w2t), (b1, b1t), (b2, b2t), (cw, cwt), (tab, table), (mask, masks)):
                sp.dma_start(dst[:], src).then_inc(consts_in, 16)
            with sp.Fori(1, RING // 2) as pair:
                for k in range(2):
                    there = place(pair, k)
                    sp.wait_ge(x_in[k], 32 * pair)
                    load(*there, k)
            with sp.Fori(0, B * PAIRS - RING // 2) as pair:
                for k in range(2):
                    done, following = place(pair, k), place(pair + RING // 2, k)
                    sp.wait_ge(added, 2 * pair + k + 2)
                    store_half(*done, k, 0)
                    sp.wait_ge(x_in[k], 32 * pair + 32 * (RING // 2))
                    store_half(*done, k, 1)
                    sp.wait_ge(x_out[k], 32 * pair + 32)
                    load(*following, k)
            with sp.Fori(B * PAIRS - RING // 2, B * PAIRS) as pair:
                places = [place(pair, k) for k in range(2)]
                for k in range(2):
                    sp.wait_ge(added, 2 * pair + k + 2)
                    store_half(*places[k], k, 0)
                    sp.wait_ge(x_out[1 - k], 32 * pair + 32 * k)
                    store_half(*places[k], k, 1)
            for k in range(2):
                sp.wait_ge(x_out[k], 32 * B * PAIRS)

        @block.gpsimd
        def _(pool):
            def rstd_of_image(n):
                pool.wait_ge(var_ready, n + 1)
                nc.gpsimd.tensor_tensor(rstd[:], var[:], nhalf[:], ALU.pow).then_inc(rstd_ready, 1)

            def add_unit(g):
                slot = ring[:, bass.ds(g % RING, 1), :].rearrange("p o (b j w) -> p (o b) j w", b=2, j=2)
                pool.wait_ge(conv_ready, g + 1)
                nc.gpsimd.tensor_tensor(slot, slot, conv[:].rearrange("p (j b w) -> p b j w", j=2, b=2),
                                        ALU.add).then_inc(added, 1)

            pool.sem_inc(added, 1)
            rstd_of_image(0)
            with pool.Fori(0, UNITS - 2) as g:
                add_unit(g)
            rstd_of_image(1)
            with pool.Fori(1, B - 1) as n:
                with pool.Fori(0, UNITS) as u:
                    add_unit(UNITS * n + u - 2)
                rstd_of_image(n + 1)
            with pool.Fori(UNITS * (B - 1) - 2, UNITS * B) as g:
                add_unit(g)

        @block.scalar
        def _(act):
            def gelu(c, par):
                for k in range(KH):
                    act.wait_ge(mm1_done, KH * c + k + 1)
                    nc.scalar.activation(hid[:, par, k], hps[:, k], ACT.Gelu,
                                         bias=b1[:, k:k + 1]).then_inc(gelu_done, 1)

            def copy_y(g):
                act.wait_ge(mm2_done, 2 * g + 2)
                nc.scalar.activation(ycopy[:].rearrange("p (b w) -> p b w", b=2), yps[:, :, W:2 * W],
                                     ACT.Identity, bias=b2[:, 0:1]).then_inc(ycopied, 1)

            def copy_z(g):
                act.wait_ge(z_ready, g + 1)
                nc.scalar.copy(zcopy[:], zps[:, 1].rearrange("p a b q -> p (a b q)")).then_inc(zcopied, 1)

            act.wait_ge(consts_in, 16 * CONSTS)
            for c in range(3):
                gelu(c, c % 2)
            copy_y(0)
            with act.Fori(1, UNITS * B - 1) as g:
                gelu(2 * g + 1, 1)
                copy_z(g - 1)
                gelu(2 * g + 2, 0)
                copy_y(g)
            last = UNITS * B - 1
            gelu(2 * last + 1, 1)
            copy_z(last - 1)
            copy_y(last)
            copy_z(last)

        @block.vector
        def _(dve):
            V = nc.vector

            def make_taps():
                dve.wait_ge(consts_in, 16 * CONSTS)
                dve.wait_ge(diag_ready, 1)
                V.tensor_copy(diag[:], zps[:, 0, 0, 0, 0:2 * TAPS]).then_inc(diag_copied, 1)
                dve.wait_ge(diag_copied, 1)
                for n in range(TAPS):
                    same = V.tensor_scalar(taps[:, n], mask[:, 0], diag[:, n:n + 1], None, ALU.mult)
                same.then_inc(taps_made, 1)
                dve.wait_ge(taps_made, 1)
                for n in range(TAPS):
                    other = V.scalar_tensor_tensor(taps[:, n], mask[:, 1], diag[:, TAPS + n:TAPS + n + 1],
                                                   taps[:, n], ALU.mult, ALU.add)
                other.then_inc(taps_made, 1)

            def statistics(pair, v, k):
                dve.wait_ge(x_in[k], 32 * pair + 32)
                for h in range(2):
                    V.bn_stats(stats[:, bass.ds(2 * v + k, 1), h * STAT:(h + 1) * STAT],
                                      ring[:, bass.ds((2 * pair + k) % RING, 1), h * CW:(h + 1) * CW])

            def normalisation(n):
                def then(ins):
                    dve.drain()

                def group_sum():
                    V.tensor_copy(swapped[0:C], part[C:P])
                    then(V.tensor_copy(swapped[C:P], part[0:C]))
                    then(V.tensor_tensor(rows[:], part[:], swapped[:], ALU.add))
                    then(V.stream_shuffle(buddy[:], rows[:], [m ^ 1 for m in range(32)]))
                    then(V.tensor_tensor(rows[:], rows[:], buddy[:], ALU.add))

                dve.drain()
                then(V.bn_aggr(mv[:], stats[:].rearrange("p u s -> p (u s)")))
                then(V.tensor_copy(part[:], mv[:, 0:1]))
                group_sum()
                then(V.tensor_scalar(mean[:], rows[:], 0.25, None, ALU.mult))
                then(V.tensor_tensor(part[:], mv[:, 0:1], mean[:], ALU.subtract))
                then(V.scalar_tensor_tensor(part[:], part[:], part[:], mv[:, 1:2], ALU.mult, ALU.add))
                group_sum()
                V.tensor_scalar(var[:], rows[:], 0.25, EPS, ALU.mult, ALU.add).then_inc(var_ready, 1)
                dve.wait_ge(rstd_ready, n + 1)
                then(V.tensor_scalar(w1s[:], w1[:], rstd[:], None, ALU.mult))
                if not (isinstance(n, int) and n == 0):
                    dve.wait_ge(mm1_done, 2 * KH * UNITS * n)
                then(V.tensor_copy(w1hi[:], w1s[:]))
                V.tensor_tensor(w1lo[:], w1s[:], w1hi[:].bitcast(F32), ALU.subtract).then_inc(scaled, 1)

            def rows_of(g, par):
                return ring[:, bass.ds(g % RING, 1), par * CW:(par + 1) * CW].rearrange("p o f -> p (o f)")

            def stage_hi(g, par, first=False):
                if not first:
                    dve.wait_ge(mm1_done, KH * (2 * g + par - 1))
                V.tensor_scalar(xhi[:, par], rows_of(g, par), mean[:], None,
                                ALU.subtract).then_inc(xhi_done, 1)

            def stage_lo(g, par):
                dve.wait_ge(xhi_done, 2 * g + par + 1)
                V.scalar_tensor_tensor(xlo[:, par], rows_of(g, par), mean[:],
                                       xhi[:, par].bitcast(F32),
                                       ALU.subtract, ALU.subtract).then_inc(staged, 1)

            def sums_over_j(g):
                dve.wait_ge(ycopied, g + 1)
                for alpha, op in enumerate((ALU.add, ALU.subtract)):
                    last = V.scalar_tensor_tensor(eo[:, alpha].rearrange("p (b w) -> p b w", b=2), yps[:, :, 0:W],
                                                  b2[:, 0:1], ycopy[:].rearrange("p (b w) -> p b w", b=2),
                                                  ALU.add, op)
                last.then_inc(y_read, 1)

            def sums_over_s(g):
                dve.wait_ge(y_read, g + 1)
                e = eo[:].rearrange("p a (q s t) -> p s a t q", s=2, t=2)
                V.tensor_tensor(vin[:, 0], e[:, 0], e[:, 1], ALU.add)
                V.tensor_tensor(vin[:, 1], e[:, 0], e[:, 1], ALU.subtract).then_inc(v_ready, 1)

            def back_over_alpha(g):
                dve.wait_ge(zcopied, g + 1)
                z1 = zcopy[:].rearrange("p (a b q) -> p a b q", a=2, b=2)
                V.tensor_tensor(gj[:, 0], zps[:, 0], z1, ALU.add)
                V.tensor_tensor(gj[:, 1], zps[:, 0], z1, ALU.subtract).then_inc(z_read, 1)

            def back_over_beta(g):
                dve.wait_ge(z_read, g + 2)
                dve.wait_ge(added, g + 1)
                o = conv[:].rearrange("p (j q s t) -> p s j t q", j=2, s=2, t=2)
                V.tensor_tensor(o[:, 0], gj[:, :, 0], gj[:, :, 1], ALU.add)
                V.tensor_tensor(o[:, 1], gj[:, :, 0], gj[:, :, 1], ALU.subtract).then_inc(conv_ready, 1)

            def unit(g, more=(), stage=True, back=True):
                sums_over_j(g)
                if stage:
                    stage_hi(g + 2, 0)
                sums_over_s(g)
                if stage:
                    stage_lo(g + 2, 0)
                if back:
                    back_over_alpha(g - 1)
                for statistic in more[:1]:
                    statistics(*statistic)
                if back:
                    back_over_beta(g - 1)
                for statistic in more[1:]:
                    statistics(*statistic)
                if stage:
                    stage_hi(g + 2, 1)
                    stage_lo(g + 2, 1)

            def inner_pair(pair, v, following, first=False):
                for k in range(2):
                    unit(2 * pair + k, more=[(pair + PAIRS, v, k)] if following else [], back=not (first and k == 0))

            def last_pair(pair, n, following):
                g = 2 * pair
                if following:
                    unit(g, more=[(pair + PAIRS, PAIRS - 1, k) for k in range(2)], stage=False)
                    normalisation(n + 1)
                    for par in range(2):
                        stage_hi(g + 2, par)
                        stage_lo(g + 2, par)
                    unit(g + 1)
                else:
                    unit(g, stage=False)
                    unit(g + 1, stage=False)

            dve.sem_inc(z_read, 1)
            V.memset(nhalf[:], -0.5)
            make_taps()
            with dve.Fori(0, PAIRS) as pair:
                for k in range(2):
                    statistics(pair, pair, k)
            normalisation(0)
            for g in range(2):
                for par in range(2):
                    stage_hi(g, par, first=g == 0)
                    stage_lo(g, par)
            inner_pair(0, 0, True, first=True)
            with dve.Fori(1, PAIRS - 1) as v:
                inner_pair(v, v, True)
            last_pair(PAIRS - 1, 0, True)
            with dve.Fori(1, B - 1) as n:
                with dve.Fori(0, PAIRS - 1) as v:
                    inner_pair(PAIRS * n + v, v, True)
                last_pair(PAIRS * n + PAIRS - 1, n, True)
            with dve.Fori(0, PAIRS - 1) as v:
                inner_pair(PAIRS * (B - 1) + v, v, False)
            last_pair(PAIRS * B - 1, B - 1, False)
            dve.wait_ge(conv_ready, UNITS * B - 1)
            back_over_alpha(UNITS * B - 1)
            back_over_beta(UNITS * B - 1)

        @block.tensor
        def _(pe):
            T = nc.tensor

            def mm1(c, par):
                pe.wait_ge(staged, c + 1)
                for k in range(KH):
                    if not (isinstance(c, int) and c == 0):
                        pe.wait_ge(gelu_done, KH * (c - 1) + k + 1)
                    for n, (a, b) in enumerate(((w1hi, xhi), (w1lo, xhi), (w1hi, xlo))):
                        for i in range(NI):
                            rows = slice(i * C, (i + 1) * C)
                            last = T.matmul(hps[:, k, i], a[rows, k * P:(k + 1) * P], b[rows, par],
                                            start=n == 0, stop=n == 2)
                    last.then_inc(mm1_done, 1)

            def mm2(c, par):
                pe.wait_ge(gelu_done, KH * c + KH)
                for k in range(KH):
                    for i in range(NI):
                        last = T.matmul(yps[i * C:(i + 1) * C, par], w2[:, k], hid[:, par, k, i],
                                        start=k == 0, stop=k == KH - 1)
                last.then_inc(mm2_done, 1)

            def conv_matmuls(g):
                pe.wait_ge(v_ready, g + 1)
                pe.wait_ge(z_read, g + 1)
                for al in range(2):
                    for be in range(2):
                        for to in range(2):
                            for t in range(2):
                                last = T.matmul(zps[:, al, be, to], taps[:, al * 8 + be * 4 + t * 2 + to],
                                                vin[:, be, al, t], start=t == 0, stop=t == 1)
                last.then_inc(z_ready, 1)

            pe.wait_ge(consts_in, 16 * CONSTS)
            for i in range(NI):
                last = T.matmul(zps[i * C:(i + 1) * C, 0, 0, 0, 0:2 * TAPS], cw[:], tab[:, i], start=True, stop=True)
            last.then_inc(diag_ready, 1)

            pe.wait_ge(scaled, 1)
            mm1(0, 0)
            mm1(1, 1)
            mm2(0, 0)
            mm1(2, 0)
            mm2(1, 1)
            pe.wait_ge(taps_made, 2)
            with pe.Fori(1, UNITS * B - 1) as g:
                mm1(2 * g + 1, 1)
                pe.wait_ge(y_read, g)
                mm2(2 * g, 0)
                conv_matmuls(g - 1)
                pe.wait_ge(scaled, (g + 1) // UNITS + 1)
                mm1(2 * g + 2, 0)
                mm2(2 * g + 1, 1)
            last_unit = UNITS * B - 1
            mm1(2 * last_unit + 1, 1)
            pe.wait_ge(y_read, last_unit)
            mm2(2 * last_unit, 0)
            conv_matmuls(last_unit - 1)
            mm2(2 * last_unit + 1, 1)
            conv_matmuls(last_unit)


def kernel(x, L0_conv_w1, L0_conv_b1, L0_conv_w2, L0_conv_b2, L0_conv_cweight):
    import concourse.bacc as bacc
    from concourse.bass_utils import run_bass_kernel_spmd

    w1t = np.asarray(L0_conv_w1).T
    eye = np.eye(P, dtype=np.float32)
    arrays = {
        "x": np.asarray(x),
        "w1t": np.concatenate([w1t] * NI),
        "b1t": np.asarray(L0_conv_b1).reshape(KH, P).T,
        "w2t": np.asarray(L0_conv_w2).T.reshape(KH, P, C).transpose(1, 0, 2),
        "b2t": np.concatenate([np.asarray(L0_conv_b2)] * NI)[:, None],
        "cwt": np.asarray(L0_conv_cweight).transpose(0, 1, 3, 2).reshape(24, C),
        "table": filter_tables().transpose(1, 0, 2).astype(np.float32),
        "masks": np.stack([eye, np.roll(eye, C, axis=1)], axis=1),
    }
    arrays = {name: np.ascontiguousarray(a) for name, a in arrays.items()}
    nc = bacc.Bacc("TRN2", target_bir_lowering=False, num_devices=1)
    args = [nc.dram_tensor(name, a.shape, mybir.dt.from_np(a.dtype), kind="ExternalInput").ap()
            for name, a in arrays.items()]
    out = nc.dram_tensor("out", (B, C, H, W), F32, kind="ExternalOutput").ap()
    program(nc, *args, out)
    result = run_bass_kernel_spmd(nc, [arrays], core_ids=[0])
    return result.results[0]["out"]
```

```python
from contextlib import ExitStack

import numpy as np

import concourse.bass as bass
from concourse import mybir

F32 = mybir.dt.float32
F32R = mybir.dt.float32r
ALU = mybir.AluOpType
ACT = mybir.ActivationFunctionType

B, C, H, W, HID = 8, 64, 256, 256, 256
PATCH = 4
GROUPS = 32
EPS = 1e-5
P = 128
KH = HID // P
NI = 2
ROWS = 2 * PATCH
UW = ROWS // NI * W
CW = UW // 2
UNITS = H // ROWS
PAIRS = UNITS // 2
RING = UNITS + 4
NQ = 2 * (W // PATCH)
STAT = 6
CONSTS = 7
LAG = 3
TAPS = 16


def filter_tables():
    table = np.zeros((NI, 24, 2 * TAPS))
    r = np.arange(PATCH)
    for u in range(PATCH):
        for v in range(PATCH // 2 + 1):
            for z in range(2):
                angle = 2 * np.pi * (u * r[:, None] + v * r[None, :]) / PATCH
                taps = (np.cos(angle) if z == 0 else -np.sin(angle)) / PATCH**2
                if v == 1:
                    taps = 2 * taps
                for n in range(TAPS):
                    al, be, t, to = (n >> 3) & 1, (n >> 2) & 1, (n >> 1) & 1, n & 1
                    for i in range(NI):
                        for other in range(2):
                            io = i ^ other
                            d, e = (io - i) & 1, (to - t) & 1
                            sign = (-1) ** (al * (io < i) + be * (to < t))
                            k = sum((-1) ** (al * a + be * s) * taps[d + 2 * a, e + 2 * s]
                                    for a in range(2) for s in range(2))
                            table[i, u * 6 + v * 2 + z, other * TAPS + n] = sign * k / 4
    return np.round(table * 64) / 64


def program(nc, x, w1t, b1t, w2t, b2t, cwt, table, masks, out):
    ctx = ExitStack()
    with ctx:
        def sb(name, shape, dt=F32):
            return ctx.enter_context(nc.sbuf_tensor(name, shape, dt))

        def ps(name, shape):
            return ctx.enter_context(nc.psum_tensor(name, shape, F32))

        def sem(name):
            return ctx.enter_context(nc.semaphore(name))

        ring = sb("ring", [P, RING, UW])
        xcut = sb("xcut", [P, 2, NI, CW], F32R)
        hid = sb("hid", [P, 2, KH, NI, CW])
        ycopy = sb("ycopy", [P, 2 * W])
        eo = sb("eo", [P, 2, UW // 2])
        vin = sb("vin", [P, 2, 2, 2, NQ])
        zcopy = sb("zcopy", [P, UW // 2])
        gj = sb("gj", [P, 2, 2, 2, NQ])
        conv = sb("conv", [P, UW])
        taps = sb("taps", [P, TAPS, P])
        w1 = sb("w1", [P, HID])
        w1s = sb("w1s", [P, HID])
        w1hi = sb("w1hi", [P, HID], F32R)
        w1lo = sb("w1lo", [P, HID], F32R)
        w2 = sb("w2", [P, KH, C])
        b1 = sb("b1", [P, KH])
        b2 = sb("b2", [P, 1])
        cw = sb("cw", [24, C])
        tab = sb("tab", [24, NI, 2 * TAPS])
        mask = sb("mask", [P, 2, P])
        diag = sb("diag", [P, 2 * TAPS])
        stats = sb("stats", [P, UNITS, 2 * STAT])
        mv = sb("mv", [P, 2])
        part = sb("part", [P, 1])
        swapped = sb("swapped", [P, 1])
        rows = sb("rows", [P, 1])
        buddy = sb("buddy", [P, 1])
        mean = sb("mean", [P, 1])
        nmean = sb("nmean", [P, 1])
        var = sb("var", [P, 1])
        rstd = sb("rstd", [P, 1])
        nhalf = sb("nhalf", [P, 1])

        hps = ps("hps", [P, KH, NI, CW])
        yps = ps("yps", [P, 2, CW])
        zps = ps("zps", [P, 2, 2, 2, NQ])

        consts_in = sem("consts_in")
        x_in = [sem("x_in0"), sem("x_in1")]
        x_out = [sem("x_out0"), sem("x_out1")]
        diag_ready = sem("diag_ready")
        diag_copied = sem("diag_copied")
        taps_made = sem("taps_made")
        staged = sem("staged")
        scaled = sem("scaled")
        mm1_done = sem("mm1_done")
        gelu_done = sem("gelu_done")
        mm2_done = sem("mm2_done")
        ycopied = sem("ycopied")
        y_read = sem("y_read")
        v_ready = sem("v_ready")
        z_ready = sem("z_ready")
        zcopied = sem("zcopied")
        z_read = sem("z_read")
        conv_ready = sem("conv_ready")
        added = sem("added")
        xhi_done = sem("xhi_done")
        nmean_ready = sem("nmean_ready")
        var_ready = sem("var_ready")
        rstd_ready = sem("rstd_ready")

        x_v = x.rearrange("n c (u r i) w -> n u i c r w", r=ROWS // NI, i=NI)
        out_v = out.rearrange("n c (u r i) w -> n u i c r w", r=ROWS // NI, i=NI)

        block = ctx.enter_context(nc.Block())

        @block.sync
        def _(sp):
            def place(pair, k):
                values = (pair // PAIRS, 2 * (pair % PAIRS) + k, (2 * pair + k) % RING)
                return [v if isinstance(v, int) else sp.snap(v) for v in values]

            def rows_of_ring(slot, i):
                return ring[i * C:(i + 1) * C, bass.ds(slot, 1), :].rearrange("c o (r w) -> c (o r) w", w=W)

            def load(n, u, slot, k):
                for i in range(NI):
                    sp.dma_start(rows_of_ring(slot, i), x_v[n, u, i]).then_inc(x_in[k], 16)

            def store_half(n, u, slot, k, i):
                sp.dma_start(out_v[n, u, i], rows_of_ring(slot, i)).then_inc(x_out[k], 16)

            for k in range(2):
                load(*place(0, k), k)
            for dst, src in ((w1, w1t), (w2, w2t), (b1, b1t), (b2, b2t), (cw, cwt), (tab, table), (mask, masks)):
                sp.dma_start(dst[:], src).then_inc(consts_in, 16)
            with sp.Fori(1, RING // 2) as pair:
                for k in range(2):
                    there = place(pair, k)
                    sp.wait_ge(x_in[k], 32 * pair)
                    load(*there, k)
            with sp.Fori(0, B * PAIRS - RING // 2) as pair:
                for k in range(2):
                    done, following = place(pair, k), place(pair + RING // 2, k)
                    sp.wait_ge(added, 2 * pair + k + 2)
                    store_half(*done, k, 0)
                    sp.wait_ge(x_in[k], 32 * pair + 32 * (RING // 2))
                    store_half(*done, k, 1)
                    sp.wait_ge(x_out[k], 32 * pair + 32)
                    load(*following, k)
            with sp.Fori(B * PAIRS - RING // 2, B * PAIRS) as pair:
                places = [place(pair, k) for k in range(2)]
                for k in range(2):
                    sp.wait_ge(added, 2 * pair + k + 2)
                    store_half(*places[k], k, 0)
                    sp.wait_ge(x_out[1 - k], 32 * pair + 32 * k)
                    store_half(*places[k], k, 1)
            for k in range(2):
                sp.wait_ge(x_out[k], 32 * B * PAIRS)

        @block.gpsimd
        def _(pool):
            def rstd_of_image(n):
                pool.wait_ge(var_ready, n + 1)
                nc.gpsimd.tensor_tensor(rstd[:], var[:], nhalf[:], ALU.pow).then_inc(rstd_ready, 1)

            def add_unit(g):
                slot = ring[:, bass.ds(g % RING, 1), :].rearrange("p o (b j w) -> p (o b) j w", b=2, j=2)
                pool.wait_ge(conv_ready, g + 1)
                nc.gpsimd.tensor_tensor(slot, slot, conv[:].rearrange("p (j b w) -> p b j w", j=2, b=2),
                                        ALU.add).then_inc(added, 1)

            pool.sem_inc(added, 1)
            rstd_of_image(0)
            with pool.Fori(0, UNITS - LAG) as g:
                add_unit(g)
            rstd_of_image(1)
            with pool.Fori(1, B - 1) as n:
                with pool.Fori(0, UNITS) as u:
                    add_unit(UNITS * n + u - LAG)
                rstd_of_image(n + 1)
            with pool.Fori(UNITS * (B - 1) - LAG, UNITS * B) as g:
                add_unit(g)

        @block.scalar
        def _(act):
            def gelu(c, par):
                for k in range(KH):
                    act.wait_ge(mm1_done, KH * c + k + 1)
                    nc.scalar.activation(hid[:, par, k], hps[:, k], ACT.Gelu,
                                         bias=b1[:, k:k + 1]).then_inc(gelu_done, 1)

            def copy_y(g):
                act.wait_ge(mm2_done, 2 * g + 2)
                nc.scalar.activation(ycopy[:].rearrange("p (b w) -> p b w", b=2), yps[:, :, W:2 * W],
                                     ACT.Identity, bias=b2[:, 0:1]).then_inc(ycopied, 1)

            def copy_z(g):
                act.wait_ge(z_ready, g + 1)
                nc.scalar.copy(zcopy[:], zps[:, 1].rearrange("p a b q -> p (a b q)")).then_inc(zcopied, 1)

            def stage_hi(g, par):
                slot = ring[:, bass.ds(g % RING, 1), par * CW:(par + 1) * CW].rearrange("p o f -> p (o f)")
                for i in range(NI):
                    rows = slice(i * C, (i + 1) * C)
                    last = nc.scalar.activation(xcut[rows, par, i], slot[rows], ACT.Identity, bias=nmean[rows, 0:1])
                last.then_inc(xhi_done, 1)

            act.wait_ge(consts_in, 16 * CONSTS)
            act.wait_ge(nmean_ready, 1)
            for par in range(2):
                stage_hi(0, par)
            gelu(0, 0)
            stage_hi(1, 0)
            gelu(1, 1)
            stage_hi(1, 1)
            gelu(2, 0)
            copy_y(0)
            stage_hi(2, 0)
            with act.Fori(1, UNITS * B - 2) as g:
                gelu(2 * g + 1, 1)
                stage_hi(g + 1, 1)
                gelu(2 * g + 2, 0)
                copy_y(g)
                act.wait_ge(nmean_ready, (g + 2) // UNITS + 1)
                stage_hi(g + 2, 0)
                copy_z(g - 1)
            last = UNITS * B - 1
            gelu(2 * last - 1, 1)
            stage_hi(last, 1)
            gelu(2 * last, 0)
            copy_y(last - 1)
            copy_z(last - 2)
            gelu(2 * last + 1, 1)
            copy_y(last)
            copy_z(last - 1)
            copy_z(last)

        @block.vector
        def _(dve):
            V = nc.vector

            def make_taps():
                dve.wait_ge(consts_in, 16 * CONSTS)
                dve.wait_ge(diag_ready, 1)
                V.tensor_copy(diag[:], zps[:, 0, 0, 0, 0:2 * TAPS]).then_inc(diag_copied, 1)
                dve.wait_ge(diag_copied, 1)
                for n in range(TAPS):
                    same = V.tensor_scalar(taps[:, n], mask[:, 0], diag[:, n:n + 1], None, ALU.mult)
                same.then_inc(taps_made, 1)
                dve.wait_ge(taps_made, 1)
                for n in range(TAPS):
                    other = V.scalar_tensor_tensor(taps[:, n], mask[:, 1], diag[:, TAPS + n:TAPS + n + 1],
                                                   taps[:, n], ALU.mult, ALU.add)
                other.then_inc(taps_made, 1)

            def statistics(pair, v, k):
                dve.wait_ge(x_in[k], 32 * pair + 32)
                for h in range(2):
                    V.bn_stats(stats[:, bass.ds(2 * v + k, 1), h * STAT:(h + 1) * STAT],
                                      ring[:, bass.ds((2 * pair + k) % RING, 1), h * CW:(h + 1) * CW])

            def then(ins):
                dve.drain()

            def moments(n):
                def group_sum():
                    V.tensor_copy(swapped[0:C], part[C:P])
                    then(V.tensor_copy(swapped[C:P], part[0:C]))
                    then(V.tensor_tensor(rows[:], part[:], swapped[:], ALU.add))
                    then(V.stream_shuffle(buddy[:], rows[:], [m ^ 1 for m in range(32)]))
                    then(V.tensor_tensor(rows[:], rows[:], buddy[:], ALU.add))

                dve.drain()
                then(V.bn_aggr(mv[:], stats[:].rearrange("p u s -> p (u s)")))
                then(V.tensor_copy(part[:], mv[:, 0:1]))
                group_sum()
                then(V.tensor_scalar(mean[:], rows[:], 0.25, None, ALU.mult))
                then(V.tensor_tensor(part[:], mv[:, 0:1], mean[:], ALU.subtract))
                then(V.scalar_tensor_tensor(part[:], part[:], part[:], mv[:, 1:2], ALU.mult, ALU.add))
                group_sum()
                V.tensor_scalar(nmean[:], mean[:], -1.0, None, ALU.mult).then_inc(nmean_ready, 1)
                V.tensor_scalar(var[:], rows[:], 0.25, EPS, ALU.mult, ALU.add).then_inc(var_ready, 1)

            def scale_w1(n):
                dve.wait_ge(rstd_ready, n + 1)
                then(V.tensor_scalar(w1s[:], w1[:], rstd[:], None, ALU.mult))
                if not (isinstance(n, int) and n == 0):
                    dve.wait_ge(mm1_done, 2 * KH * UNITS * n)
                then(V.tensor_copy(w1hi[:], w1s[:]))
                V.tensor_tensor(w1lo[:], w1s[:], w1hi[:].bitcast(F32), ALU.subtract).then_inc(scaled, 1)

            def rows_of(g, par):
                return ring[:, bass.ds(g % RING, 1), par * CW:(par + 1) * CW].rearrange("p o f -> p (o f)")

            def stage_lo(g, par):
                dve.wait_ge(xhi_done, 2 * g + par + 1)
                for i in range(NI):
                    rows, others = slice(i * C, (i + 1) * C), slice((1 - i) * C, (2 - i) * C)
                    last = V.scalar_tensor_tensor(xcut[others, par, i], rows_of(g, par)[rows], nmean[rows],
                                                  xcut[rows, par, i].bitcast(F32), ALU.add, ALU.subtract)
                last.then_inc(staged, 1)

            def sums_over_j(g):
                dve.wait_ge(ycopied, g + 1)
                if not (isinstance(g, int) and g == 0):
                    dve.wait_ge(v_ready, g)
                for alpha, op in enumerate((ALU.add, ALU.subtract)):
                    last = V.scalar_tensor_tensor(eo[:, alpha].rearrange("p (b w) -> p b w", b=2), yps[:, :, 0:W],
                                                  b2[:, 0:1], ycopy[:].rearrange("p (b w) -> p b w", b=2),
                                                  ALU.add, op)
                last.then_inc(y_read, 1)

            def sums_over_s(g):
                dve.wait_ge(y_read, g + 1)
                if not (isinstance(g, int) and g == 0):
                    dve.wait_ge(z_ready, g)
                e = eo[:].rearrange("p a (q s t) -> p s a t q", s=2, t=2)
                V.tensor_tensor(vin[:, 0], e[:, 0], e[:, 1], ALU.add)
                V.tensor_tensor(vin[:, 1], e[:, 0], e[:, 1], ALU.subtract).then_inc(v_ready, 1)

            def back_over_alpha(g):
                dve.wait_ge(zcopied, g + 1)
                if not (isinstance(g, int) and g == 0):
                    dve.wait_ge(conv_ready, g)
                z1 = zcopy[:].rearrange("p (a b q) -> p a b q", a=2, b=2)
                V.tensor_tensor(gj[:, 0], zps[:, 0], z1, ALU.add)
                V.tensor_tensor(gj[:, 1], zps[:, 0], z1, ALU.subtract).then_inc(z_read, 1)

            def back_over_beta(g):
                dve.wait_ge(z_read, g + 2)
                dve.wait_ge(added, g + 1)
                o = conv[:].rearrange("p (j q s t) -> p s j t q", j=2, s=2, t=2)
                V.tensor_tensor(o[:, 0], gj[:, :, 0], gj[:, :, 1], ALU.add)
                V.tensor_tensor(o[:, 1], gj[:, :, 0], gj[:, :, 1], ALU.subtract).then_inc(conv_ready, 1)

            def way_in(g):
                sums_over_j(g)
                sums_over_s(g)

            def way_back(g):
                back_over_alpha(g)
                back_over_beta(g)

            def unit(pair, k, v=None, staging=True, back=True):
                g = 2 * pair + k
                sums_over_j(g)
                if staging:
                    stage_lo(g + 2, 0)
                sums_over_s(g)
                if back:
                    way_back(g - 1)
                if v is not None:
                    statistics(pair + PAIRS, v, k)
                if staging:
                    stage_lo(g + 2, 1)

            def last_pair(pair, n, following):
                g = 2 * pair
                if following:
                    for k in range(2):
                        statistics(pair + PAIRS, PAIRS - 1, k)
                    moments(n + 1)
                way_in(g)
                if following:
                    scale_w1(n + 1)
                    for par in range(2):
                        stage_lo(g + 2, par)
                way_back(g - 1)
                unit(pair, 1, staging=following)

            dve.sem_inc(z_read, 1)
            V.memset(nhalf[:], -0.5)
            make_taps()
            with dve.Fori(0, PAIRS) as pair:
                for k in range(2):
                    statistics(pair, pair, k)
            moments(0)
            scale_w1(0)
            for g in range(2):
                for par in range(2):
                    stage_lo(g, par)
            for k in range(2):
                unit(0, k, 0, back=k == 1)
            with dve.Fori(1, PAIRS - 1) as v:
                for k in range(2):
                    unit(v, k, v)
            last_pair(PAIRS - 1, 0, True)
            with dve.Fori(1, B - 1) as n:
                with dve.Fori(0, PAIRS - 1) as v:
                    for k in range(2):
                        unit(PAIRS * n + v, k, v)
                last_pair(PAIRS * n + PAIRS - 1, n, True)
            with dve.Fori(0, PAIRS - 1) as v:
                for k in range(2):
                    unit(PAIRS * (B - 1) + v, k)
            last_pair(PAIRS * B - 1, B - 1, False)
            way_back(UNITS * B - 1)

        @block.tensor
        def _(pe):
            T = nc.tensor

            def mm1(c, par):
                pe.wait_ge(staged, c + 1)
                for k in range(KH):
                    if not (isinstance(c, int) and c == 0):
                        pe.wait_ge(gelu_done, KH * (c - 1) + k + 1)
                    for w in (w1hi, w1lo):
                        for i in range(NI):
                            last = T.matmul(hps[:, k, i], w[:, k * P:(k + 1) * P], xcut[:, par, i],
                                            start=w is w1hi, stop=w is w1lo)
                    last.then_inc(mm1_done, 1)

            def mm2(c, par):
                pe.wait_ge(gelu_done, KH * c + KH)
                for k in range(KH):
                    for i in range(NI):
                        last = T.matmul(yps[i * C:(i + 1) * C, par], w2[:, k], hid[:, par, k, i],
                                        start=k == 0, stop=k == KH - 1)
                last.then_inc(mm2_done, 1)

            def conv_matmuls(g):
                pe.wait_ge(v_ready, g + 1)
                pe.wait_ge(z_read, g + 1)
                for al in range(2):
                    for be in range(2):
                        for to in range(2):
                            for t in range(2):
                                last = T.matmul(zps[:, al, be, to], taps[:, al * 8 + be * 4 + t * 2 + to],
                                                vin[:, be, al, t], start=t == 0, stop=t == 1)
                last.then_inc(z_ready, 1)

            pe.wait_ge(consts_in, 16 * CONSTS)
            for i in range(NI):
                last = T.matmul(zps[i * C:(i + 1) * C, 0, 0, 0, 0:2 * TAPS], cw[:], tab[:, i], start=True, stop=True)
            last.then_inc(diag_ready, 1)

            pe.wait_ge(scaled, 1)
            mm1(0, 0)
            mm1(1, 1)
            mm2(0, 0)
            mm1(2, 0)
            mm2(1, 1)
            pe.wait_ge(taps_made, 2)
            with pe.Fori(1, UNITS * B - 1) as g:
                mm1(2 * g + 1, 1)
                pe.wait_ge(y_read, g)
                mm2(2 * g, 0)
                pe.wait_ge(scaled, (g + 1) // UNITS + 1)
                mm1(2 * g + 2, 0)
                mm2(2 * g + 1, 1)
                conv_matmuls(g - 1)
            last_unit = UNITS * B - 1
            mm1(2 * last_unit + 1, 1)
            pe.wait_ge(y_read, last_unit)
            mm2(2 * last_unit, 0)
            mm2(2 * last_unit + 1, 1)
            conv_matmuls(last_unit - 1)
            conv_matmuls(last_unit)


def kernel(x, L0_conv_w1, L0_conv_b1, L0_conv_w2, L0_conv_b2, L0_conv_cweight):
    import concourse.bacc as bacc
    from concourse.bass_utils import run_bass_kernel_spmd

    w1t = np.asarray(L0_conv_w1).T
    eye = np.eye(P, dtype=np.float32)
    arrays = {
        "x": np.asarray(x),
        "w1t": np.concatenate([w1t] * NI),
        "b1t": np.asarray(L0_conv_b1).reshape(KH, P).T,
        "w2t": np.asarray(L0_conv_w2).T.reshape(KH, P, C).transpose(1, 0, 2),
        "b2t": np.concatenate([np.asarray(L0_conv_b2)] * NI)[:, None],
        "cwt": np.asarray(L0_conv_cweight).transpose(0, 1, 3, 2).reshape(24, C),
        "table": filter_tables().transpose(1, 0, 2).astype(np.float32),
        "masks": np.stack([eye, np.roll(eye, C, axis=1)], axis=1),
    }
    arrays = {name: np.ascontiguousarray(a) for name, a in arrays.items()}
    nc = bacc.Bacc("TRN2", target_bir_lowering=False, num_devices=1)
    args = [nc.dram_tensor(name, a.shape, mybir.dt.from_np(a.dtype), kind="ExternalInput").ap()
            for name, a in arrays.items()]
    out = nc.dram_tensor("out", (B, C, H, W), F32, kind="ExternalOutput").ap()
    program(nc, *args, out)
    result = run_bass_kernel_spmd(nc, [arrays], core_ids=[0])
    return result.results[0]["out"]
```

```python
from contextlib import ExitStack

import numpy as np

import concourse.bass as bass
from concourse import mybir

F32 = mybir.dt.float32
F32R = mybir.dt.float32r
ALU = mybir.AluOpType
ACT = mybir.ActivationFunctionType

B, C, H, W, HID = 8, 64, 256, 256, 256
PATCH = 4
GROUPS = 32
EPS = 1e-5
P = 128
KH = HID // P
NI = 2
ROWS = 2 * PATCH
UW = ROWS // NI * W
CW = UW // 2
UNITS = H // ROWS
PAIRS = UNITS // 2
RING = UNITS + 4
NQ = 2 * (W // PATCH)
STAT = 6
CONSTS = 7
LAG = 2
MATRICES = [(al, be, other) for al in range(2) for be in range(2) for other in range(2)]
TAPS = len(MATRICES)


def filter_tables():
    table = np.zeros((NI, 24, 2 * TAPS))
    r = np.arange(PATCH)
    for u in range(PATCH):
        for v in range(PATCH // 2 + 1):
            for z in range(2):
                angle = 2 * np.pi * (u * r[:, None] + v * r[None, :]) / PATCH
                taps = (np.cos(angle) if z == 0 else -np.sin(angle)) / PATCH**2
                if v == 1:
                    taps = 2 * taps
                for n, (al, be, e) in enumerate(MATRICES):
                    for i in range(NI):
                        for other in range(2):
                            io = i ^ other
                            d = (io - i) & 1
                            sign = (-1) ** (al * (io < i))
                            k = sum((-1) ** (al * a + be * s) * taps[d + 2 * a, e + 2 * s]
                                    for a in range(2) for s in range(2))
                            table[i, u * 6 + v * 2 + z, other * TAPS + n] = sign * k / 4
    return np.round(table * 64) / 64


def program(nc, x, w1t, b1t, w2t, b2t, cwt, table, masks, out):
    ctx = ExitStack()
    with ctx:
        def sb(name, shape, dt=F32):
            return ctx.enter_context(nc.sbuf_tensor(name, shape, dt))

        def ps(name, shape):
            return ctx.enter_context(nc.psum_tensor(name, shape, F32))

        def sem(name):
            return ctx.enter_context(nc.semaphore(name))

        ring = sb("ring", [P, RING, UW])
        xcut = sb("xcut", [P, 2, NI, CW], F32R)
        hid = sb("hid", [P, 2, KH, NI, CW])
        half = sb("half", [P, UW // 2])
        eo = sb("eo", [P, 2, UW // 2])
        v0 = sb("v0", [P, 2, 2, NQ])
        vhi0 = sb("vhi0", [P, 2, 2, NQ], F32R)
        vlo0 = sb("vlo0", [P, 2, 2, NQ], F32R)
        vhi1 = sb("vhi1", [P, 2, 3, NQ], F32R)
        vlo1 = sb("vlo1", [P, 2, 3, NQ], F32R)
        gj = sb("gj", [P, 2, 2, 2, NQ])
        conv = sb("conv", [P, UW])
        tapshi = sb("tapshi", [P, TAPS, P], F32R)
        tapslo = sb("tapslo", [P, TAPS, P], F32R)
        w1 = sb("w1", [P, HID])
        w1hi = sb("w1hi", [P, HID], F32R)
        w1lo = sb("w1lo", [P, HID], F32R)
        w2 = sb("w2", [P, KH, C])
        b1 = sb("b1", [P, KH])
        b2 = sb("b2", [P, 1])
        stats = sb("stats", [P, UNITS, 2 * STAT])
        mv = sb("mv", [P, 2])
        other = sb("other", [P, 2])
        joined = sb("joined", [P, 2])
        group = sb("group", [P, 2])
        dist = sb("dist", [P, 1])
        nmean = sb("nmean", [P, 1])
        var = sb("var", [P, 1])
        rstd = sb("rstd", [P, 1])
        nhalf = sb("nhalf", [P, 1])

        scratch = hid[:].rearrange("p a k i w -> p (a k i w)")
        at = [0]

        def cut(shape):
            size = int(np.prod(shape[1:]))
            at[0] += size
            piece = scratch[0:shape[0], at[0] - size:at[0]]
            names = "abc"[:len(shape) - 1]
            return piece.rearrange(f"p ({' '.join(names)}) -> p {' '.join(names)}", **dict(zip(names, shape[1:])))

        taps = cut([P, TAPS, P])
        mask = cut([P, 2, P])
        cw = cut([24, C])
        tab = cut([24, NI, 2 * TAPS])
        diag = cut([P, 2 * TAPS])

        hps = ps("hps", [P, KH, NI, CW])
        yps = ps("yps", [P, 2, CW])
        zps = ps("zps", [P, 2, 2, 2, NQ])

        consts_in = sem("consts_in")
        x_first = [sem("x_first0"), sem("x_first1")]
        x_in = [sem("x_in0"), sem("x_in1")]
        x_out = [sem("x_out0"), sem("x_out1")]
        diag_ready = sem("diag_ready")
        diag_copied = sem("diag_copied")
        taps_made = sem("taps_made")
        staged = sem("staged")
        scaled = sem("scaled")
        mm1_done = sem("mm1_done")
        gelu_done = sem("gelu_done")
        mm2_done = sem("mm2_done")
        ycopied = sem("ycopied")
        y_read = sem("y_read")
        v0_ready = sem("v0_ready")
        v_ready = sem("v_ready")
        vhi_ready = sem("vhi_ready")
        v_read = sem("v_read")
        vlo_ready = sem("vlo_ready")
        z_ready = sem("z_ready")
        zcopied = sem("zcopied")
        z_read = sem("z_read")
        conv_ready = sem("conv_ready")
        added = sem("added")
        xhi_done = sem("xhi_done")
        nmean_ready = sem("nmean_ready")
        var_ready = sem("var_ready")
        rstd_ready = sem("rstd_ready")

        x_v = x.rearrange("n c (u r i) w -> n u i c r w", r=ROWS // NI, i=NI)
        first_v = x.rearrange("n c (p r i) w -> n p i c r w", r=2 * ROWS // NI, i=NI)[0]
        out_v = out.rearrange("n c (u r i) w -> n u i c r w", r=ROWS // NI, i=NI)

        block = ctx.enter_context(nc.Block())

        @block.sync
        def _(sp):
            def place(pair, k):
                values = (pair // PAIRS, 2 * (pair % PAIRS) + k, (2 * pair + k) % RING)
                return [v if isinstance(v, int) else sp.snap(v) for v in values]

            def rows_of_ring(slot, i):
                return ring[i * C:(i + 1) * C, bass.ds(slot, 1), :].rearrange("c o (r w) -> c (o r) w", w=W)

            def load(n, u, slot, k):
                for i in range(NI):
                    sp.dma_start(rows_of_ring(slot, i), x_v[n, u, i]).then_inc(x_in[k], 16)

            def store_half(n, u, slot, k, i):
                sp.dma_start(out_v[n, u, i], rows_of_ring(slot, i)).then_inc(x_out[k], 16)

            def load_pair(pair, k):
                for i in range(NI):
                    rows = ring[i * C:(i + 1) * C, bass.ds(2 * pair, 2), :].rearrange("c u (r w) -> c (u r) w", w=W)
                    sp.dma_start(rows, first_v[pair, i]).then_inc(x_first[k], 16)

            for k in range(2):
                load_pair(k, k)
            for dst, src in ((w1[:], w1t), (w2[:], w2t), (b1[:], b1t), (b2[:], b2t), (cw, cwt), (tab, table), (mask, masks)):
                sp.dma_start(dst, src).then_inc(consts_in, 16)
            with sp.Fori(1, PAIRS // 2) as two:
                for k in range(2):
                    sp.wait_ge(x_first[k], 32 * two)
                    load_pair(2 * two + k, k)
            for pair in range(PAIRS, RING // 2):
                for k in range(2):
                    if pair > PAIRS:
                        sp.wait_ge(x_in[k], 32 * (pair - PAIRS))
                    load(*place(pair, k), k)
            with sp.Fori(0, B * PAIRS - RING // 2) as pair:
                for k in range(2):
                    done, following = place(pair, k), place(pair + RING // 2, k)
                    sp.wait_ge(added, 2 * pair + k + 2)
                    store_half(*done, k, 0)
                    sp.wait_ge(x_in[k], 32 * pair + 32 * (RING // 2 - PAIRS))
                    store_half(*done, k, 1)
                    sp.wait_ge(x_out[k], 32 * pair + 32)
                    load(*following, k)
            with sp.Fori(B * PAIRS - RING // 2, B * PAIRS) as pair:
                places = [place(pair, k) for k in range(2)]
                for k in range(2):
                    sp.wait_ge(added, 2 * pair + k + 2)
                    store_half(*places[k], k, 0)
                    sp.wait_ge(x_out[1 - k], 32 * pair + 32 * k)
                    store_half(*places[k], k, 1)
            for k in range(2):
                sp.wait_ge(x_out[k], 32 * B * PAIRS)

        @block.gpsimd
        def _(pool):
            def rstd_of_image(n):
                pool.wait_ge(var_ready, n + 1)
                nc.gpsimd.tensor_tensor(rstd[:], var[:], nhalf[:], ALU.pow).then_inc(rstd_ready, 1)

            def cut_v(g):
                v1 = eo[:].rearrange("p a (q s t) -> p s a t q", s=2, t=2)[:, 0]
                pool.wait_ge(vhi_ready, 2 * g + 1)
                nc.gpsimd.tensor_tensor(vlo0[:], v0[:], vhi0[:].bitcast(F32), ALU.subtract)
                pool.wait_ge(vhi_ready, 2 * g + 2)
                nc.gpsimd.tensor_tensor(vlo1[:, :, 1:3], v1, vhi1[:, :, 1:3].bitcast(F32),
                                        ALU.subtract).then_inc(v_read, 1)

            def add_unit(g):
                slot = ring[:, bass.ds(g % RING, 1), :].rearrange("p o (b j w) -> p (o b) j w", b=2, j=2)
                pool.wait_ge(conv_ready, g + 1)
                nc.gpsimd.tensor_tensor(slot, slot, conv[:].rearrange("p (j b w) -> p b j w", j=2, b=2),
                                        ALU.add).then_inc(added, 1)

            def unit(g):
                cut_v(g)
                add_unit(g - 1)

            pool.sem_inc(added, 1)
            rstd_of_image(0)
            cut_v(0)
            with pool.Fori(1, UNITS - LAG) as g:
                unit(g)
            rstd_of_image(1)
            with pool.Fori(1, B - 1) as n:
                with pool.Fori(0, UNITS) as u:
                    unit(UNITS * n + u - LAG)
                rstd_of_image(n + 1)
            with pool.Fori(UNITS * (B - 1) - LAG, UNITS * B) as g:
                unit(g)
            add_unit(UNITS * B - 1)

        @block.scalar
        def _(act):
            def gelu(c, par, k):
                act.wait_ge(mm1_done, KH * c + k + 1)
                nc.scalar.activation(hid[:, par, k], hps[:, k], ACT.Gelu,
                                     bias=b1[:, k:k + 1]).then_inc(gelu_done, 1)

            def copy_y(g):
                act.wait_ge(mm2_done, 2 * g + 2)
                if not (isinstance(g, int) and g == 0):
                    act.wait_ge(z_read, g)
                nc.scalar.activation(half[:].rearrange("p (b w) -> p b w", b=2), yps[:, :, W:2 * W],
                                     ACT.Identity, bias=b2[:, 0:1]).then_inc(ycopied, 1)

            def copy_z(g):
                act.wait_ge(z_ready, g + 1)
                act.wait_ge(y_read, min(g + 2, UNITS * B) if isinstance(g, int) else g + 2)
                nc.scalar.copy(half[:], zps[:, 1].rearrange("p a b q -> p (a b q)")).then_inc(zcopied, 1)

            def cut_v0(g):
                act.wait_ge(v0_ready, g + 1)
                nc.scalar.copy(vhi0[:], v0[:]).then_inc(vhi_ready, 1)

            def cut_v1(g):
                act.wait_ge(v_ready, g + 1)
                v1 = eo[:].rearrange("p a (q s t) -> p s a t q", s=2, t=2)[:, 0]
                nc.scalar.copy(vhi1[:, :, 1:3], v1)
                nc.scalar.mul(vhi1[:, :, 0], v1[:, :, 1], -1.0).then_inc(vhi_ready, 1)

            def negate_vlo(g):
                act.wait_ge(v_read, g + 1)
                nc.scalar.mul(vlo1[:, :, 0], vlo1[:, :, 2].bitcast(F32), -1.0).then_inc(vlo_ready, 1)

            def stage_hi(g, par):
                slot = ring[:, bass.ds(g % RING, 1), par * CW:(par + 1) * CW].rearrange("p o f -> p (o f)")
                for i in range(NI):
                    rows = slice(i * C, (i + 1) * C)
                    last = nc.scalar.activation(xcut[rows, par, i], slot[rows], ACT.Identity, bias=nmean[rows, 0:1])
                last.then_inc(xhi_done, 1)

            def unit(g, first=False):
                copy_y(g)
                gelu(2 * g + 2, 0, 1)
                stage_hi(g + 2, 0)
                if not first:
                    copy_z(g - 1)
                gelu(2 * g + 3, 1, 0)
                cut_v0(g)
                gelu(2 * g + 3, 1, 1)
                cut_v1(g)
                stage_hi(g + 2, 1)
                gelu(2 * g + 4, 0, 0)
                negate_vlo(g)

            def last_but_one(g, n):
                copy_y(g)
                gelu(2 * g + 2, 0, 1)
                act.wait_ge(nmean_ready, n + 2)
                stage_hi(g + 2, 0)
                copy_z(g - 1)
                for k in range(KH):
                    gelu(2 * g + 3, 1, k)
                cut_v0(g)
                cut_v1(g)
                stage_hi(g + 2, 1)
                gelu(2 * g + 4, 0, 0)
                negate_vlo(g)

            act.wait_ge(consts_in, 16 * CONSTS)
            act.wait_ge(nmean_ready, 1)
            act.wait_ge(taps_made, 4)
            for par in range(2):
                stage_hi(0, par)
            for c in range(2):
                for k in range(KH):
                    gelu(c, c, k)
                stage_hi(1, c)
            gelu(2, 0, 0)
            unit(0, first=True)
            with act.Fori(1, UNITS - 2) as g:
                unit(g)
            last_but_one(UNITS - 2, 0)
            with act.Fori(1, B - 1) as n:
                with act.Fori(0, UNITS - 1) as u:
                    unit(UNITS * n + u - 1)
                last_but_one(UNITS * n + UNITS - 2, n)
            with act.Fori(UNITS * (B - 1) - 1, UNITS * B - 2) as g:
                unit(g)
            last = UNITS * B - 1
            copy_y(last - 1)
            gelu(2 * last, 0, 1)
            copy_z(last - 2)
            gelu(2 * last + 1, 1, 0)
            cut_v0(last - 1)
            gelu(2 * last + 1, 1, 1)
            cut_v1(last - 1)
            negate_vlo(last - 1)
            copy_y(last)
            copy_z(last - 1)
            cut_v0(last)
            cut_v1(last)
            negate_vlo(last)
            copy_z(last)

        @block.vector
        def _(dve):
            V = nc.vector

            def make_taps():
                dve.wait_ge(consts_in, 16 * CONSTS)
                dve.wait_ge(diag_ready, 1)
                V.tensor_copy(diag, zps[:, 0, 0, 0, 0:2 * TAPS]).then_inc(diag_copied, 1)
                dve.wait_ge(diag_copied, 1)
                for n in range(TAPS):
                    same = V.tensor_scalar(taps[:, n], mask[:, 0], diag[:, n:n + 1], None, ALU.mult)
                same.then_inc(taps_made, 1)
                dve.wait_ge(taps_made, 1)
                for n in range(TAPS):
                    other = V.scalar_tensor_tensor(taps[:, n], mask[:, 1], diag[:, TAPS + n:TAPS + n + 1],
                                                   taps[:, n], ALU.mult, ALU.add)
                other.then_inc(taps_made, 1)
                dve.wait_ge(taps_made, 2)
                V.tensor_copy(tapshi[:], taps).then_inc(taps_made, 1)
                dve.wait_ge(taps_made, 3)
                V.tensor_tensor(tapslo[:], taps, tapshi[:].bitcast(F32), ALU.subtract).then_inc(taps_made, 1)

            def statistics_of(u, slot):
                for h in range(2):
                    V.bn_stats(stats[:, bass.ds(u, 1), h * STAT:(h + 1) * STAT],
                               ring[:, bass.ds(slot, 1), h * CW:(h + 1) * CW])

            def statistics(pair, v, k):
                dve.wait_ge(x_in[k], 32 * (pair - PAIRS) + 32)
                statistics_of(2 * v + k, (2 * pair + k) % RING)

            def then(ins):
                dve.drain()

            def moments(n):
                def join(out, one, two, scale):
                    V.tensor_scalar(dist[:], one[:, 0:1], two[:, 0:1], scale, ALU.subtract, ALU.mult)
                    then(V.tensor_tensor(out[:], one[:], two[:], ALU.add))
                    then(V.scalar_tensor_tensor(out[:, 1:2], dist[:], dist[:], out[:, 1:2], ALU.mult, ALU.add))

                dve.drain()
                then(V.bn_aggr(mv[:], stats[:].rearrange("p u s -> p (u s)")))
                V.tensor_copy(other[0:C], mv[C:P])
                then(V.tensor_copy(other[C:P], mv[0:C]))
                join(joined, mv, other, 0.5 ** 0.5)
                then(V.stream_shuffle(other[:], joined[:], [m ^ 1 for m in range(32)]))
                join(group, joined, other, 0.5)
                V.tensor_scalar(nmean[:], group[:, 0:1], -0.25, None, ALU.mult).then_inc(nmean_ready, 1)
                V.tensor_scalar(var[:], group[:, 1:2], 0.25, EPS, ALU.mult, ALU.add).then_inc(var_ready, 1)

            def scale_w1(n):
                dve.wait_ge(rstd_ready, n + 1)
                if not (isinstance(n, int) and n == 0):
                    dve.wait_ge(mm1_done, 2 * KH * UNITS * n)
                then(V.tensor_scalar(w1hi[:], w1[:], rstd[:], None, ALU.mult))
                V.scalar_tensor_tensor(w1lo[:], w1[:], rstd[:], w1hi[:].bitcast(F32), ALU.mult,
                                       ALU.subtract).then_inc(scaled, 1)

            def rows_of(g, par):
                return ring[:, bass.ds(g % RING, 1), par * CW:(par + 1) * CW].rearrange("p o f -> p (o f)")

            def stage_lo(g, par):
                dve.wait_ge(xhi_done, 2 * g + par + 1)
                for i in range(NI):
                    rows, others = slice(i * C, (i + 1) * C), slice((1 - i) * C, (2 - i) * C)
                    last = V.scalar_tensor_tensor(xcut[others, par, i], rows_of(g, par)[rows], nmean[rows],
                                                  xcut[rows, par, i].bitcast(F32), ALU.add, ALU.subtract)
                last.then_inc(staged, 1)

            def sums_over_j(g):
                dve.wait_ge(ycopied, g + 1)
                if not (isinstance(g, int) and g == 0):
                    dve.wait_ge(v_read, g)
                for alpha, op in enumerate((ALU.add, ALU.subtract)):
                    last = V.scalar_tensor_tensor(eo[:, alpha].rearrange("p (b w) -> p b w", b=2), yps[:, :, 0:W],
                                                  b2[:, 0:1], half[:].rearrange("p (b w) -> p b w", b=2),
                                                  ALU.add, op)
                last.then_inc(y_read, 1)

            def sums_over_s(g):
                dve.wait_ge(y_read, g + 1)
                e = eo[:].rearrange("p a (q s t) -> p s a t q", s=2, t=2)
                V.tensor_tensor(v0[:], e[:, 0], e[:, 1], ALU.add).then_inc(v0_ready, 1)
                dve.wait_ge(v0_ready, g + 1)
                V.tensor_tensor(e[:, 0], e[:, 0], e[:, 1], ALU.subtract).then_inc(v_ready, 1)

            def back_over_alpha(g):
                dve.wait_ge(zcopied, g + 1)
                if not (isinstance(g, int) and g == 0):
                    dve.wait_ge(conv_ready, g)
                z1 = half[:].rearrange("p (a b q) -> p a b q", a=2, b=2)
                V.tensor_tensor(gj[:, 0], zps[:, 0], z1, ALU.add)
                V.tensor_tensor(gj[:, 1], zps[:, 0], z1, ALU.subtract).then_inc(z_read, 1)

            def back_over_beta(g):
                dve.wait_ge(z_read, g + 2)
                dve.wait_ge(added, g + 1)
                o = conv[:].rearrange("p (j q s t) -> p s j t q", j=2, s=2, t=2)
                V.tensor_tensor(o[:, 0], gj[:, :, 0], gj[:, :, 1], ALU.add)
                V.tensor_tensor(o[:, 1], gj[:, :, 0], gj[:, :, 1], ALU.subtract).then_inc(conv_ready, 1)

            def unit(pair, k, v=None, staging=True, back=True):
                g = 2 * pair + k
                sums_over_j(g)
                sums_over_s(g)
                if staging:
                    stage_lo(g + 2, 0)
                if back:
                    back_over_alpha(g - 1)
                if v is not None:
                    statistics(pair + PAIRS + k, v + k, 1 - k)
                if back:
                    back_over_beta(g - 1)
                if staging:
                    stage_lo(g + 2, 1)

            def last_pair(pair, n, following):
                g = 2 * pair
                if following:
                    statistics(pair + PAIRS, PAIRS - 1, 1)
                    moments(n + 1)
                sums_over_j(g)
                if following:
                    scale_w1(n + 1)
                    stage_lo(g + 2, 0)
                sums_over_s(g)
                back_over_alpha(g - 1)
                back_over_beta(g - 1)
                if following:
                    stage_lo(g + 2, 1)
                unit(pair, 1, staging=following)

            dve.sem_inc(z_read, 1)
            V.memset(nhalf[:], -0.5)
            make_taps()
            with dve.Fori(0, PAIRS // 2) as two:
                for k in range(2):
                    dve.wait_ge(x_first[k], 32 * two + 32)
                    for u in range(2):
                        statistics_of(4 * two + 2 * k + u, 4 * two + 2 * k + u)
            moments(0)
            scale_w1(0)
            for g in range(2):
                for par in range(2):
                    stage_lo(g, par)
            statistics(PAIRS, 0, 0)
            for k in range(2):
                unit(0, k, 0, back=k == 1)
            with dve.Fori(1, PAIRS - 1) as v:
                for k in range(2):
                    unit(v, k, v)
            last_pair(PAIRS - 1, 0, True)
            with dve.Fori(1, B - 1) as n:
                statistics(PAIRS * n + PAIRS, 0, 0)
                with dve.Fori(0, PAIRS - 1) as v:
                    for k in range(2):
                        unit(PAIRS * n + v, k, v)
                last_pair(PAIRS * n + PAIRS - 1, n, True)
            with dve.Fori(0, PAIRS - 1) as v:
                for k in range(2):
                    unit(PAIRS * (B - 1) + v, k)
            last_pair(PAIRS * B - 1, B - 1, False)
            back_over_alpha(UNITS * B - 1)
            back_over_beta(UNITS * B - 1)

        @block.tensor
        def _(pe):
            T = nc.tensor

            def mm1(c, par):
                pe.wait_ge(staged, c + 1)
                for k in range(KH):
                    if not (isinstance(c, int) and c == 0):
                        pe.wait_ge(gelu_done, KH * (c - 1) + k + 1)
                    hidden = slice(k * P, (k + 1) * P)
                    for i in range(NI):
                        T.matmul(hps[:, k, i], w1hi[:, hidden], xcut[:, par, i], start=True, stop=False)
                    for i in range(NI):
                        rows = slice(i * C, (i + 1) * C)
                        last = T.matmul(hps[:, k, i], w1lo[rows, hidden], xcut[rows, par, i], start=False, stop=True)
                    last.then_inc(mm1_done, 1)

            def mm2(c, par):
                pe.wait_ge(gelu_done, KH * c + KH)
                for k in range(KH):
                    for i in range(NI):
                        last = T.matmul(yps[i * C:(i + 1) * C, par], w2[:, k], hid[:, par, k, i],
                                        start=k == 0, stop=k == KH - 1)
                last.then_inc(mm2_done, 1)

            def conv_matmuls(g):
                pe.wait_ge(vlo_ready, g + 1)
                pe.wait_ge(z_read, g + 1)
                for al in range(2):
                    for be in range(2):
                        hi, lo = (vhi1, vlo1) if be else (vhi0, vlo0)
                        straight, crossed = (slice(1, 3), slice(0, 2)) if be else (slice(0, 2), slice(None, None, -1))
                        terms = [(w[:, MATRICES.index((al, be, other))], v[:, al, order])
                                 for other, order in enumerate((straight, crossed))
                                 for w, v in ((tapshi, hi), (tapshi, lo), (tapslo, hi))]
                        for n, (w, v) in enumerate(terms):
                            last = T.matmul(zps[:, al, be], w, v, start=n == 0, stop=n == len(terms) - 1)
                last.then_inc(z_ready, 1)

            pe.wait_ge(consts_in, 16 * CONSTS)
            for i in range(NI):
                last = T.matmul(zps[i * C:(i + 1) * C, 0, 0, 0, 0:2 * TAPS], cw, tab[:, i], start=True, stop=True)
            last.then_inc(diag_ready, 1)

            pe.wait_ge(scaled, 1)
            mm1(0, 0)
            mm1(1, 1)
            mm2(0, 0)
            mm1(2, 0)
            mm2(1, 1)
            pe.wait_ge(taps_made, 4)
            with pe.Fori(1, UNITS * B - 1) as g:
                mm1(2 * g + 1, 1)
                pe.wait_ge(y_read, g)
                mm2(2 * g, 0)
                pe.wait_ge(scaled, (g + 1) // UNITS + 1)
                mm1(2 * g + 2, 0)
                mm2(2 * g + 1, 1)
                conv_matmuls(g - 1)
            last_unit = UNITS * B - 1
            mm1(2 * last_unit + 1, 1)
            pe.wait_ge(y_read, last_unit)
            mm2(2 * last_unit, 0)
            mm2(2 * last_unit + 1, 1)
            conv_matmuls(last_unit - 1)
            conv_matmuls(last_unit)


def kernel(x, L0_conv_w1, L0_conv_b1, L0_conv_w2, L0_conv_b2, L0_conv_cweight):
    import concourse.bacc as bacc
    from concourse.bass_utils import run_bass_kernel_spmd

    w1t = np.asarray(L0_conv_w1).T
    eye = np.eye(P, dtype=np.float32)
    arrays = {
        "x": np.asarray(x),
        "w1t": np.concatenate([w1t] * NI),
        "b1t": np.asarray(L0_conv_b1).reshape(KH, P).T,
        "w2t": np.asarray(L0_conv_w2).T.reshape(KH, P, C).transpose(1, 0, 2),
        "b2t": np.concatenate([np.asarray(L0_conv_b2)] * NI)[:, None],
        "cwt": np.asarray(L0_conv_cweight).transpose(0, 1, 3, 2).reshape(24, C),
        "table": filter_tables().transpose(1, 0, 2).astype(np.float32),
        "masks": np.stack([eye, np.roll(eye, C, axis=1)], axis=1),
    }
    arrays = {name: np.ascontiguousarray(a) for name, a in arrays.items()}
    nc = bacc.Bacc("TRN2", target_bir_lowering=False, num_devices=1)
    args = [nc.dram_tensor(name, a.shape, mybir.dt.from_np(a.dtype), kind="ExternalInput").ap()
            for name, a in arrays.items()]
    out = nc.dram_tensor("out", (B, C, H, W), F32, kind="ExternalOutput").ap()
    program(nc, *args, out)
    result = run_bass_kernel_spmd(nc, [arrays], core_ids=[0])
    return result.results[0]["out"]
```
